# Optimizing a Trainium2 kernel written in Bass

```python
import numpy as np
import jax
import jax.numpy as jnp

def _softmax(x, axis=-1):
    return jax.nn.softmax(x, axis=axis)

def _gelu(x):
    return jax.nn.gelu(x, approximate=True)

def _silu(x):
    return jax.nn.silu(x)

def _sigmoid(x):
    return jax.nn.sigmoid(x)

def _layernorm(x, axis=-1, eps=1e-05):
    m = jnp.mean(x, axis=axis, keepdims=True)
    v = jnp.var(x, axis=axis, keepdims=True)
    return (x - m) / jnp.sqrt(v + eps)

def _scatter_add(tgt, idx, src, axis=0):
    return tgt.at[idx].add(src)

def _segment_sum(src, seg, n):
    return jax.ops.segment_sum(src, seg, n)
kernel_name = 'mk_adj_ffn_d1_adj_r2_cd444f'

def setup_inputs(seed: int=0):
    np.random.seed(seed)
    _w = jnp.asarray

    def _rec_inputs():
        import jax
        import jax.numpy as jnp
        _gk = jax.random.key(seed)
        x = 7.22e-05 + 1 * jax.random.normal(jax.random.fold_in(_gk, 1), (128, 128, 128), jnp.float32)
        _a = jax.random.bernoulli(jax.random.fold_in(_gk, 2), 0.125, (128, 128, 128))
        _a = jnp.logical_or(_a, jnp.swapaxes(_a, -1, -2))
        _a = jnp.logical_or(_a, jnp.eye(128, dtype=bool))
        _af = _a.astype(jnp.float32)
        _af = _af * jax.random.uniform(jax.random.fold_in(_gk, 3), (128, 128, 128), jnp.float32, 0.05, 1)
        adj = _af
        return (x, adj)
    x, adj = _rec_inputs()

    def _L0_gnn_setup():
        import jax, jax.numpy as jnp
        import numpy as np
        MIN_VALUE = 1e-10
        key = jax.random.key(seed)
        k1, k2, k3, k4, k5 = jax.random.split(key, 5)
        B, N, F, P = (32, 512, 128, 128)
        x = jax.random.normal(k1, (B, N, F), dtype=jnp.float32)
        adjacency_matrix = jax.random.uniform(k2, (B, N, N), dtype=jnp.float32)
        bound = 1.0 / np.sqrt(F)
        W = jax.random.uniform(k3, (P, F), minval=-bound, maxval=bound, dtype=jnp.float32)
        b = jax.random.uniform(k4, (P,), minval=-bound, maxval=bound, dtype=jnp.float32)
        alpha = jax.random.uniform(k5, (1,), dtype=jnp.float32)
        return {'x': x, 'adjacency_matrix': adjacency_matrix, 'W': W, 'b': b, 'alpha': alpha}
    _L0_gnn_all = _L0_gnn_setup()
    _L0_gnn_in = {k: v for k, v in _L0_gnn_all.items() if k in ('W', 'b', 'alpha')}
    del _L0_gnn_all

    def _L0_ffn_setup():
        import jax, jax.numpy as jnp
        import numpy as np
        E = 8
        K = 2
        D = 128
        H = 256
        DOUT = 128
        EPS = 1e-05
        key = jax.random.key(seed)
        ks = jax.random.split(key, 9)
        s = 0.02
        return {'x': jax.random.normal(ks[0], (4, 4096, D), jnp.float32), 'gamma': 1.0 + 0.05 * jax.random.normal(ks[1], (D,), jnp.float32), 'beta': 0.05 * jax.random.normal(ks[2], (D,), jnp.float32), 'Wr': 0.01 * jax.random.normal(ks[3], (D, E), jnp.float32), 'br': jnp.zeros((E,), jnp.float32), 'W1': s * jax.random.normal(ks[4], (E, D, H), jnp.float32), 'b1': s * jax.random.normal(ks[5], (E, H), jnp.float32), 'W2': s * jax.random.normal(ks[6], (E, H, DOUT), jnp.float32), 'b2': s * jax.random.normal(ks[7], (E, DOUT), jnp.float32)}
    _L0_ffn_all = _L0_ffn_setup()
    _L0_ffn_in = {k: v for k, v in _L0_ffn_all.items() if k in ('gamma', 'beta', 'Wr', 'br', 'W1', 'b1', 'W2', 'b2')}
    del _L0_ffn_all
    return {'x': x, 'adj': adj, 'L0_gnn_W': _L0_gnn_in['W'], 'L0_gnn_b': _L0_gnn_in['b'], 'L0_gnn_alpha': _L0_gnn_in['alpha'], 'L0_ffn_gamma': _L0_ffn_in['gamma'], 'L0_ffn_beta': _L0_ffn_in['beta'], 'L0_ffn_Wr': _L0_ffn_in['Wr'], 'L0_ffn_br': _L0_ffn_in['br'], 'L0_ffn_W1': _L0_ffn_in['W1'], 'L0_ffn_b1': _L0_ffn_in['b1'], 'L0_ffn_W2': _L0_ffn_in['W2'], 'L0_ffn_b2': _L0_ffn_in['b2']}

def reference(x, adj, L0_gnn_W, L0_gnn_b, L0_gnn_alpha, L0_ffn_gamma, L0_ffn_beta, L0_ffn_Wr, L0_ffn_br, L0_ffn_W1, L0_ffn_b1, L0_ffn_W2, L0_ffn_b2):
    import jax
    import jax.numpy as jnp

    def _L0_gnn_ref(x, adjacency_matrix, W, b, alpha):
        import jax, jax.numpy as jnp
        import numpy as np
        MIN_VALUE = 1e-10
        deg = adjacency_matrix.sum(axis=-1)
        deg = jnp.where(deg != 0, deg, 1.0)
        d_inv_sqrt = deg ** (-0.5)
        norm_adj = d_inv_sqrt[:, :, None] * adjacency_matrix * d_inv_sqrt[:, None, :]
        alpha_eff = jnp.maximum(alpha[0], MIN_VALUE)
        N = adjacency_matrix.shape[1]
        a_plus = norm_adj + alpha_eff * jnp.eye(N, dtype=adjacency_matrix.dtype)
        h = jnp.einsum('bnm,bmf->bnf', a_plus, x)
        return jnp.einsum('bnf,pf->bnp', h, W) + b

    def _L0_ffn_ref(x, gamma, beta, Wr, br, W1, b1, W2, b2):
        import jax, jax.numpy as jnp
        import numpy as np
        E = 8
        K = 2
        D = 128
        H = 256
        DOUT = 128
        EPS = 1e-05
        mu = jnp.mean(x, axis=-1, keepdims=True)
        var = jnp.mean(jnp.square(x - mu), axis=-1, keepdims=True)
        xn = (x - mu) * jax.lax.rsqrt(var + EPS) * gamma + beta
        logits = jnp.einsum('bsd,de->bse', xn, Wr) + br
        top_vals, top_idx = jax.lax.top_k(logits, K)
        w = jax.nn.softmax(top_vals, axis=-1)
        w_full = jnp.einsum('bsk,bske->bse', w, jax.nn.one_hot(top_idx, E, dtype=w.dtype))
        y = jnp.zeros(x.shape[:-1] + (DOUT,), x.dtype)
        for e in range(E):
            h = jax.nn.gelu(jnp.einsum('bsd,dh->bsh', xn, W1[e]) + b1[e], approximate=False)
            y_e = jnp.einsum('bsh,hd->bsd', h, W2[e]) + b2[e]
            y = y + y_e * w_full[..., e, None]
        return y
    x = x + _L0_gnn_ref(_layernorm(x, axis=-1), adj, L0_gnn_W, L0_gnn_b, L0_gnn_alpha)
    x = x + _L0_ffn_ref(_layernorm(x, axis=-1), L0_ffn_gamma, L0_ffn_beta, L0_ffn_Wr, L0_ffn_br, L0_ffn_W1, L0_ffn_b1, L0_ffn_W2, L0_ffn_b2)
    return x

_drawn_inputs = setup_inputs


def setup_inputs(seed=0):
    import zlib

    import numpy as np

    out = dict(_drawn_inputs(seed))
    spreads = {'L0_ffn_br': (0.0, 0.1)}
    factors = {'L0_ffn_gamma': 8.0,
     'L0_ffn_beta': 8.0,
     'L0_ffn_Wr': 3.323,
     'L0_ffn_b1': 8.0,
     'L0_ffn_b2': 4.177}
    for name, (base, spread) in spreads.items():
        noise = np.random.default_rng([zlib.crc32(name.encode()), seed]).standard_normal(out[name].shape)
        drawn = base * np.exp(spread * noise) if base else spread * noise
        out[name] = jnp.asarray(drawn.astype(out[name].dtype))
    for name, factor in factors.items():
        out[name] = (out[name] * factor).astype(out[name].dtype)
    return out
```

```python
import math
from contextlib import ExitStack

import concourse.bass as bass
from concourse import mybir

F32 = mybir.dt.float32
F32R = mybir.dt.float32r
U32 = mybir.dt.uint32
ALU = mybir.AluOpType
ACT = mybir.ActivationFunctionType
AX = mybir.AxisListType

P = 128
T = 4
N = T * P
EPS = 1e-5
MIN_ALPHA = 1e-10


def after(group, n):
    half, parity = group
    return half + (parity + n) // 2, (parity + n) % 2


def number(group):
    return 2 * group[0] + group[1]


def build(nc, x, adj, W, b, alpha, gamma, beta, Wr, br, W1, b1, W2, b2, out):
    G = x.shape[0] // T
    E = W1.shape[0]
    C = W1.shape[2] // P
    K = E * C
    ROWS = K + E + 2
    HB = 2 * C
    PAIR = 2

    def exists(group):
        half, parity = group
        return not isinstance(half, int) or 0 <= 2 * half + parity < G

    def count(per_group, group, k):
        return per_group * number(group) + k

    x_v = x.rearrange("(g t) n f -> g n t f", t=T)
    adj_v = adj.rearrange("(g t) n m -> g n t m", t=T)
    out_v = out.rearrange("(g t) n f -> g n t f", t=T)

    ctx = ExitStack()
    with ctx:
        def sb(name, shape, dt=F32):
            return ctx.enter_context(nc.sbuf_tensor(name, shape, dt))

        def ps(name, shape):
            return ctx.enter_context(nc.psum_tensor(name, shape, F32))

        def sem(name):
            return ctx.enter_context(nc.semaphore(name))

        gates_dram = nc.dram_tensor("gates_scratch", (2, E, T, P), F32, kind="Internal").ap()

        ident = sb("ident", [P, P])
        minus_half = sb("minus_half", [P, 2 * T])
        euler = sb("euler", [P, T])
        iota_e = sb("iota_e", [P, E])
        small_rows = sb("small_rows", [P, P])
        small_cols = sb("small_cols", [P, P])
        b1_col = small_cols[:, 0:K]
        b2_col = small_cols[:, K:K + E]
        gamma_col = small_cols[:, K + E:K + E + 1]
        beta_col = small_cols[:, K + E + 1:K + E + 2]
        W_sb = sb("W_sb", [P, P])
        WT = sb("WT", [P, P])
        bias_bc = sb("bias_bc", [P, P])
        br_bc = sb("br_bc", [P, E])
        alpha_bc = sb("alpha_bc", [P, 1])
        alpha_eff = sb("alpha_eff", [P, 1])
        Wr_sb = sb("Wr_sb", [P, E])
        w_raw = sb("w_raw", [P, K * P])
        W1_hi = sb("W1_hi", [P, K * P], F32R)
        W1_lo = sb("W1_lo", [P, K * P], F32R)
        W2_hi = sb("W2_hi", [P, K * P], F32R)
        W2_lo = sb("W2_lo", [P, K * P], F32R)

        xt = sb("xt", [P, 2, T, P])
        at = sb("at", [P, 2, T, P])
        x_stats = sb("x_stats", [P, T, 6])
        x_mv = sb("x_mv", [P, T, 2])
        deg = sb("deg", [P, T])
        pow_in = sb("pow_in", [P, 2 * T])
        pow_out = sb("pow_out", [P, 2, 2 * T])
        r_d = sb("r_d", [P, T])
        alpha_deg = sb("alpha_deg", [P, T])
        xs = sb("xs", [P, T, P])
        a2 = sb("a2", [P, T, P])
        a2T = sb("a2T", [P, N])
        hT = sb("hT", [P, N])
        xb = sb("xb", [P, T, P])
        x1 = sb("x1", [P, 2, T, P])
        x1_stats = sb("x1_stats", [P, T, 6])
        x1_mv = sb("x1_mv", [P, T, 2])
        var2 = sb("var2", [P, T])
        s2 = sb("s2", [P, T])
        xc = sb("xc", [P, T, P])
        xn = sb("xn", [P, N])
        x_hi = sb("x_hi", [P, 2, N], F32R)
        x_lo = sb("x_lo", [P, 2, N], F32R)
        logits = sb("logits", [P, T, E])
        top_v = sb("top_v", [P, T, 8])
        top_i = sb("top_i", [P, T, 8], U32)
        top_f = sb("top_f", [P, T, 2])
        gap = sb("gap", [P, T])
        z = sb("z", [P, T])
        z1 = sb("z1", [P, T])
        g1 = sb("g1", [P, T])
        g2 = sb("g2", [P, T])
        hot1 = sb("hot1", [P, T, E])
        hot2 = sb("hot2", [P, T, E])
        gates = sb("gates", [P, P])
        gatesT = sb("gatesT", [P, P])
        gate_bc = sb("gate_bc", [P, 2, E, N])

        h32 = sb("h32", [P, 2, C, N])
        h_hi = sb("h_hi", [P, 4, C, N], F32R)
        h_lo = sb("h_lo", [P, 4, C, N], F32R)
        gated = sb("gated", [P, 2, N])
        acc = sb("acc", [P, 2, N])
        out_sb = sb("out_sb", [P, 2, T, P])

        ps_h = [ps(f"ps_h{k}", [P, N]) for k in range(HB)]
        ps_y = [ps(f"ps_y{k}", [P, N]) for k in range(2)]
        ps_a = ps("ps_a", [P, N])
        ps_b = ps("ps_b", [P, N])

        small_loaded = sem("small_loaded")
        w1_loaded, w2_loaded = sem("w1_loaded"), sem("w2_loaded")
        x_loaded = [sem(f"x_loaded{k}") for k in range(2)]
        adj_loaded = [sem(f"adj_loaded{k}") for k in range(2)]
        zeroed, ident_ready, consts_ready = sem("zeroed"), sem("ident_ready"), sem("consts_ready")
        setup_ps, setup_sb = sem("setup_ps"), sem("setup_sb")
        w_hi_done, w_split = sem("w_hi_done"), sem("w_split")
        alpha_ready = sem("alpha_ready")
        x_stats_ready, x_mv_ready = sem("x_stats_ready"), sem("x_mv_ready")
        deg_ready, pow_in_ready, pow_out_ready = sem("deg_ready"), sem("pow_in_ready"), sem("pow_out_ready")
        scales_ready = sem("scales_ready")
        xs_ready, a2_ready, xb_ready = sem("xs_ready"), sem("a2_ready"), sem("xb_ready")
        a2T_ps, a2T_ready = sem("a2T_ps"), sem("a2T_ready")
        hT_ps, hT_ready = sem("hT_ps"), sem("hT_ready")
        conv_ps, x1_ready = sem("conv_ps"), sem("x1_ready")
        x1_stats_ready, x1_mv_ready = sem("x1_stats_ready"), sem("x1_mv_ready")
        var2_ready, s2_ready, xc_ready = sem("var2_ready"), sem("s2_ready"), sem("xc_ready")
        xcT_ps, xn_ready, x_hi_ready, x_lo_ready = sem("xcT_ps"), sem("xn_ready"), sem("x_hi_ready"), sem("x_lo_ready")
        logits_ps, logits_ready = sem("logits_ps"), sem("logits_ready")
        top_v_ready, top_ready = sem("top_v_ready"), sem("top_ready")
        z_ready, z1_ready, g1_ready, g2_ready = sem("z_ready"), sem("z1_ready"), sem("g1_ready"), sem("g2_ready")
        top_f_ready, hot_ready, gates_ready = sem("top_f_ready"), sem("hot_ready"), sem("gates_ready")
        gatesT_ps, gatesT_ready = sem("gatesT_ps"), sem("gatesT_ready")
        gates_stored = sem("gates_stored")
        gate_loaded = [sem(f"gate_loaded{k}") for k in range(E // PAIR)]
        hidden_ps, gelu_done = sem("hidden_ps"), sem("gelu_done")
        h_hi_ready, h_lo_ready = sem("h_hi_ready"), sem("h_lo_ready")
        y_ps, gated_ready, acc_ready = sem("y_ps"), sem("gated_ready"), sem("acc_ready")
        yT_ps, out_ready = sem("yT_ps"), sem("out_ready")
        stored = [sem(f"stored{k}") for k in range(2)]

        block = ctx.enter_context(nc.Block())

        def run(eng, start, body):
            start()
            body((0, 0))
            body((0, 1))
            with eng.Fori(1, G // 2 - 1) as half:
                body((half, 0))
                body((half, 1))
            body((G // 2 - 1, 0))
            body((G // 2 - 1, 1))

        @block.sync
        def _(sp):
            def load(g):
                p = g[1]
                if exists(after(g, -2)):
                    sp.wait_ge(xs_ready, count(1, after(g, -2), 1))
                    sp.wait_ge(a2_ready, count(1, after(g, -2), 1))
                    sp.wait_ge(xb_ready, count(1, after(g, -2), 1))
                sp.dma_start(xt[:, p], x_v[number(g)]).then_inc(x_loaded[p], 16)
                sp.dma_start(at[:, p], adj_v[number(g)]).then_inc(adj_loaded[p], 16)

            def spread_gates(g):
                p = g[1]
                sp.wait_ge(gatesT_ready, count(1, g, 1))
                if exists(after(g, -1)):
                    for k in range(E // PAIR):
                        sp.wait_ge(gate_loaded[k], count(16, after(g, -1), 16))
                sp.dma_start(gates_dram[p].rearrange("e t n -> t e n"), gatesT[0:T * E, :]).then_inc(gates_stored, 16)
                sp.wait_ge(gates_stored, count(16, g, 16))
                if exists(after(g, -2)):
                    sp.wait_ge(gated_ready, count(E, after(g, -2), E))
                for k in range(E // PAIR):
                    src = gates_dram[p, PAIR * k:PAIR * (k + 1)].rearrange("e t n -> (e t n)").partition_broadcast(P)
                    sp.dma_start(gate_bc[:, p, PAIR * k:PAIR * (k + 1), :].rearrange("p e n -> p (e n)"), src) \
                        .then_inc(gate_loaded[k], 16)

            def store(g):
                sp.wait_ge(out_ready, count(1, g, 1))
                sp.dma_start(out_v[number(g)], out_sb[:, g[1]]).then_inc(stored[g[1]], 16)

            def start():
                load((0, 0))
                sp.dma_start(W_sb[:, :], W).then_inc(small_loaded, 16)
                sp.dma_start(bias_bc[:, :], b.partition_broadcast(P)).then_inc(small_loaded, 16)
                sp.dma_start(br_bc[:, :], br.partition_broadcast(P)).then_inc(small_loaded, 16)
                sp.dma_start(alpha_bc[:, :], alpha.partition_broadcast(P)).then_inc(small_loaded, 16)
                sp.dma_start(Wr_sb[:, :], Wr).then_inc(small_loaded, 16)
                sp.wait_ge(zeroed, 1)
                sp.dma_start(small_rows[0:K, :], b1.rearrange("e (c p) -> (e c) p", p=P)).then_inc(small_loaded, 16)
                sp.dma_start(small_rows[K:K + E, :], b2).then_inc(small_loaded, 16)
                sp.dma_start(small_rows[K + E:K + E + 1, :], gamma.partition_broadcast(1)).then_inc(small_loaded, 16)
                sp.dma_start(small_rows[K + E + 1:ROWS, :], beta.partition_broadcast(1)).then_inc(small_loaded, 16)
                sp.dma_start(w_raw[:, :].rearrange("p (e h) -> p e h", e=E),
                             W1.rearrange("e d h -> d e h")).then_inc(w1_loaded, 16)
                load((0, 1))
                sp.wait_ge(w_split, 1)
                sp.dma_start(w_raw[:, :].rearrange("p (k o) -> p k o", o=P),
                             W2.rearrange("e (c p) o -> p (e c) o", p=P)).then_inc(w2_loaded, 16)
                spread_gates((0, 0))

            def body(g):
                if exists(after(g, 2)):
                    load(after(g, 2))
                if exists(after(g, -1)):
                    store(after(g, -1))
                if exists(after(g, 1)):
                    spread_gates(after(g, 1))

            run(sp, start, body)
            store((G // 2 - 1, 1))
            for p in range(2):
                sp.wait_ge(stored[p], 16 * (G // 2))

        SMALL_LOADS = 9 * 16

        @block.gpsimd
        def _(pool):
            def degree_pow(g):
                pool.wait_ge(pow_in_ready, count(1, g, 1))
                if exists(after(g, -2)):
                    pool.wait_ge(x1_ready, count(1, after(g, -2), 1))
                nc.gpsimd.tensor_tensor(pow_out[:, g[1], :], pow_in[:, :], minus_half[:, :], ALU.pow) \
                    .then_inc(pow_out_ready, 1)
                if exists(after(g, -1)):
                    pool.wait_ge(xs_ready, count(1, after(g, -1), 1))
                    pool.wait_ge(a2_ready, count(1, after(g, -1), 1))
                pool.wait_ge(pow_out_ready, count(1, g, 1))
                nc.gpsimd.tensor_tensor(r_d[:, :], pow_out[:, g[1], 0:T], pow_out[:, g[1], T:2 * T], ALU.mult)
                nc.gpsimd.tensor_scalar(alpha_deg[:, :], pow_in[:, T:2 * T], alpha_eff[:, 0:1], None, ALU.mult) \
                    .then_inc(scales_ready, 1)

            def add_bias(g):
                pool.wait_ge(x_loaded[g[1]], 16 * g[0] + 16)
                if exists(after(g, -1)):
                    pool.wait_ge(x1_ready, count(1, after(g, -1), 1))
                nc.gpsimd.tensor_tensor(xb[:, :, :], xt[:, g[1]], bias_bc[:, None, :].broadcast_to([P, T, P]), ALU.add) \
                    .then_inc(xb_ready, 1)

            def norm_pow(g):
                pool.wait_ge(var2_ready, count(1, g, 1))
                if exists(after(g, -1)):
                    pool.wait_ge(xc_ready, count(1, after(g, -1), 1))
                nc.gpsimd.tensor_tensor(s2[:, :], var2[:, :], minus_half[:, 0:T], ALU.pow).then_inc(s2_ready, 1)

            def gate(g):
                pool.wait_ge(consts_ready, 1)
                pool.wait_ge(top_ready, count(1, g, 1))
                nc.gpsimd.tensor_copy(top_f[:, :, :], top_i[:, :, 0:2]).then_inc(top_f_ready, 1)
                nc.gpsimd.tensor_tensor(z[:, :], euler[:, :], gap[:, :], ALU.pow).then_inc(z_ready, 1)
                pool.wait_ge(consts_ready, 1)
                pool.wait_ge(z_ready, count(1, g, 1))
                nc.gpsimd.tensor_scalar(z1[:, :], z[:, :], 1.0, None, ALU.add).then_inc(z1_ready, 1)
                pool.wait_ge(g1_ready, count(1, g, 1))
                nc.gpsimd.tensor_tensor(g2[:, :], g1[:, :], z[:, :], ALU.mult).then_inc(g2_ready, 1)
                pool.wait_ge(consts_ready, 1)
                pool.wait_ge(top_f_ready, count(1, g, 1))
                pool.wait_ge(g2_ready, count(1, g, 1))
                for t in range(T):
                    nc.gpsimd.tensor_scalar(hot1[:, t, :], iota_e[:, :], top_f[:, t, 0:1], g1[:, t:t + 1],
                                            ALU.is_equal, ALU.mult)
                    last = nc.gpsimd.tensor_scalar(hot2[:, t, :], iota_e[:, :], top_f[:, t, 1:2], g2[:, t:t + 1],
                                                   ALU.is_equal, ALU.mult)
                last.then_inc(hot_ready, 1)
                pool.wait_ge(hot_ready, count(1, g, 1))
                if exists(after(g, -1)):
                    pool.wait_ge(gatesT_ps, count(1, after(g, -1), 1))
                nc.gpsimd.tensor_tensor(gates[:, 0:T * E].rearrange("p (t e) -> p t e", e=E), hot1[:, :, :],
                                        hot2[:, :, :], ALU.add).then_inc(gates_ready, 1)

            def accumulate(g, e):
                pool.wait_ge(gated_ready, count(E, g, e + 1))
                if e > 1:
                    pool.wait_ge(acc_ready, count(E - 1, g, e - 1))
                nc.gpsimd.tensor_tensor(acc[:, g[1], :], acc[:, g[1], :], gated[:, e % 2, :], ALU.add) \
                    .then_inc(acc_ready, 1)

            def start():
                nc.gpsimd.memset(ident[:, :], 0.0).then_inc(ident_ready, 1)
                nc.gpsimd.memset(small_rows[:, :], 0.0).then_inc(zeroed, 1)
                nc.gpsimd.memset(gates[:, :], 0.0)
                nc.gpsimd.memset(minus_half[:, :], -0.5)
                nc.gpsimd.memset(euler[:, :], math.e)
                nc.gpsimd.iota(iota_e[:, :], [[1, E]], base=0, channel_multiplier=0,
                               allow_small_or_imprecise_dtypes=True).then_inc(consts_ready, 1)
                pool.wait_ge(ident_ready, 1)
                nc.gpsimd.affine_select(out=ident[:, :], in_=ident[:, :], compare_op=ALU.not_equal, fill=1.0,
                                        base=0, pattern=[[-1, P]], channel_multiplier=1).then_inc(ident_ready, 1)
                pool.wait_ge(small_loaded, SMALL_LOADS)
                nc.gpsimd.tensor_scalar(alpha_eff[:, :], alpha_bc[:, :], MIN_ALPHA, None, ALU.max).then_inc(alpha_ready, 1)
                pool.wait_ge(alpha_ready, 1)
                pool.wait_ge(consts_ready, 1)
                degree_pow((0, 0))
                add_bias((0, 0))
                norm_pow((0, 0))
                gate((0, 0))
                degree_pow((0, 1))
                add_bias((0, 1))

            def body(g):
                for s in range(E):
                    if s == 0:
                        if exists(after(g, -1)):
                            accumulate(after(g, -1), E - 1)
                    elif s >= 2:
                        accumulate(g, s - 1)
                    if s == 2 and exists(after(g, 1)):
                        norm_pow(after(g, 1))
                    if s == 5 and exists(after(g, 1)):
                        gate(after(g, 1))
                    if s == 6 and exists(after(g, 2)):
                        degree_pow(after(g, 2))
                        add_bias(after(g, 2))

            run(pool, start, body)
            accumulate((G // 2 - 1, 1), E - 1)

        @block.scalar
        def _(act):
            def hidden(g, e):
                for c in range(C):
                    k = C * e + c
                    act.wait_ge(hidden_ps, count(K, g, k + 1))
                    if c == 0 and (e >= 2 or exists(after(g, -1))):
                        act.wait_ge(h_lo_ready, count(E, g, e - 1))
                    nc.scalar.activation(h32[:, e % 2, c, :], ps_h[k % HB][:, :], ACT.Gelu, bias=b1_col[:, k:k + 1]) \
                        .then_inc(gelu_done, 1)
                act.wait_ge(gelu_done, count(K, g, C * (e + 1)))
                if e >= 4 or exists(after(g, -1)):
                    act.wait_ge(y_ps, count(E, g, e - 3))
                nc.scalar.activation(h_hi[:, e % 4], h32[:, e % 2], ACT.Copy).then_inc(h_hi_ready, 1)

            def evacuate_a2T(g):
                act.wait_ge(a2T_ps, count(1, g, 1))
                if exists(after(g, -1)):
                    act.wait_ge(hT_ps, count(1, after(g, -1), 1))
                nc.scalar.activation(a2T[:, :], ps_a[:, :], ACT.Copy).then_inc(a2T_ready, 1)

            def evacuate_hT(g):
                act.wait_ge(hT_ps, count(1, g, 1))
                if exists(after(g, -1)):
                    act.wait_ge(conv_ps, count(1, after(g, -1), 1))
                nc.scalar.activation(hT[:, :], ps_b[:, :], ACT.Copy).then_inc(hT_ready, 1)

            def scale_xn(g):
                act.wait_ge(xcT_ps, count(1, g, 1))
                if exists(after(g, -1)):
                    act.wait_ge(logits_ps, count(1, after(g, -1), 1))
                    act.wait_ge(x_lo_ready, count(1, after(g, -1), 1))
                if exists(after(g, -2)):
                    act.wait_ge(hidden_ps, count(K, after(g, -2), K))
                nc.scalar.activation(x_hi[:, g[1], :], ps_a[:, :], ACT.Identity, bias=beta_col, scale=gamma_col) \
                    .then_inc(x_hi_ready, 1)
                nc.scalar.activation(xn[:, :], ps_a[:, :], ACT.Identity, bias=beta_col, scale=gamma_col) \
                    .then_inc(xn_ready, 1)

            def evacuate_gatesT(g):
                act.wait_ge(gatesT_ps, count(1, g, 1))
                if exists(after(g, -1)):
                    act.wait_ge(gates_stored, count(16, after(g, -1), 16))
                nc.scalar.activation(gatesT[:, :], ps_a[:, 0:P], ACT.Copy).then_inc(gatesT_ready, 1)

            def start():
                act.wait_ge(setup_ps, 1)
                nc.scalar.activation(small_cols[:, :], ps_a[:, 0:P], ACT.Copy)
                nc.scalar.activation(WT[:, :], ps_a[:, P:2 * P], ACT.Copy).then_inc(setup_sb, 1)
                act.wait_ge(setup_sb, 1)
                evacuate_a2T((0, 0))
                evacuate_hT((0, 0))
                scale_xn((0, 0))
                evacuate_gatesT((0, 0))
                hidden((0, 0), 0)
                hidden((0, 0), 1)

            def body(g):
                for s in range(E):
                    if s + 2 < E:
                        hidden(g, s + 2)
                    elif exists(after(g, 1)):
                        hidden(after(g, 1), s + 2 - E)
                    if exists(after(g, 1)):
                        step = {0: evacuate_a2T, 1: evacuate_hT, 4: scale_xn, 7: evacuate_gatesT}.get(s)
                        if step:
                            step(after(g, 1))

            run(act, start, body)

        @block.vector
        def _(dve):
            def split_weights(loaded, n, hi, lo):
                dve.wait_ge(loaded, 16)
                nc.vector.tensor_copy(hi[:, :], w_raw[:, :]).then_inc(w_hi_done, 1)
                dve.wait_ge(w_hi_done, n)
                nc.vector.tensor_tensor(lo[:, :], w_raw[:, :], hi[:, :].bitcast(F32), ALU.subtract).then_inc(w_split, 1)

            def front_stats(g):
                p = g[1]
                dve.wait_ge(x_loaded[p], 16 * g[0] + 16)
                for t in range(T):
                    last = nc.vector.bn_stats(x_stats[:, t, :], xt[:, p, t, :])
                last.then_inc(x_stats_ready, 1)
                dve.wait_ge(adj_loaded[p], 16 * g[0] + 16)
                dve.wait_ge(x_stats_ready, count(1, g, 1))
                nc.vector.reduce_sum(deg[:, :], at[:, p], AX.X).then_inc(deg_ready, 1)
                for t in range(T):
                    last = nc.vector.bn_aggr(x_mv[:, t, :], x_stats[:, t, :])
                last.then_inc(x_mv_ready, 1)
                dve.wait_ge(deg_ready, count(1, g, 1))
                if exists(after(g, -1)):
                    dve.wait_ge(scales_ready, count(1, after(g, -1), 1))
                nc.vector.scalar_tensor_tensor(pow_in[:, T:2 * T], deg[:, :], 0.0, deg[:, :], ALU.is_equal, ALU.add)
                dve.wait_ge(x_mv_ready, count(1, g, 1))
                nc.vector.tensor_scalar(pow_in[:, 0:T], x_mv[:, :, 1], EPS, None, ALU.add).then_inc(pow_in_ready, 1)

            def front_scale(g):
                p = g[1]
                dve.wait_ge(scales_ready, count(1, g, 1))
                if exists(after(g, -1)):
                    dve.wait_ge(a2T_ps, count(1, after(g, -1), 1))
                for t in range(T):
                    last = nc.vector.scalar_tensor_tensor(a2[:, t, :], ident[:, :], alpha_deg[:, t:t + 1],
                                                          at[:, p, t, :], ALU.mult, ALU.add)
                last.then_inc(a2_ready, 1)
                if exists(after(g, -1)):
                    dve.wait_ge(hT_ps, count(1, after(g, -1), 1))
                for t in range(T):
                    last = nc.vector.tensor_scalar(xs[:, t, :], xt[:, p, t, :], x_mv[:, t, 0:1], r_d[:, t:t + 1],
                                                   ALU.subtract, ALU.mult)
                last.then_inc(xs_ready, 1)

            def residual(g):
                p = g[1]
                dve.wait_ge(xb_ready, count(1, g, 1))
                if exists(after(g, -2)):
                    dve.wait_ge(out_ready, count(1, after(g, -2), 1))
                dve.wait_ge(conv_ps, count(1, g, 1))
                for t in range(T):
                    last = nc.vector.scalar_tensor_tensor(x1[:, p, t, :], ps_b[:, t * P:(t + 1) * P],
                                                          pow_out[:, p, T + t:T + t + 1], xb[:, t, :],
                                                          ALU.mult, ALU.add)
                last.then_inc(x1_ready, 1)
                dve.wait_ge(x1_ready, count(1, g, 1))
                for t in range(T):
                    last = nc.vector.bn_stats(x1_stats[:, t, :], x1[:, p, t, :])
                last.then_inc(x1_stats_ready, 1)
                dve.wait_ge(ident_ready, 2)
                dve.wait_ge(x1_stats_ready, count(1, g, 1))
                for t in range(T):
                    last = nc.vector.bn_aggr(x1_mv[:, t, :], x1_stats[:, t, :])
                last.then_inc(x1_mv_ready, 1)
                dve.wait_ge(x1_mv_ready, count(1, g, 1))
                if exists(after(g, -1)):
                    dve.wait_ge(s2_ready, count(1, after(g, -1), 1))
                nc.vector.tensor_scalar(var2[:, :], x1_mv[:, :, 1], 1.0 + EPS, EPS * EPS, ALU.mult, ALU.add) \
                    .then_inc(var2_ready, 1)

            def center(g):
                dve.wait_ge(s2_ready, count(1, g, 1))
                if exists(after(g, -1)):
                    dve.wait_ge(xcT_ps, count(1, after(g, -1), 1))
                for t in range(T):
                    last = nc.vector.tensor_scalar(xc[:, t, :], x1[:, g[1], t, :], x1_mv[:, t, 0:1], s2[:, t:t + 1],
                                                   ALU.subtract, ALU.mult)
                last.then_inc(xc_ready, 1)

            def split_x(g):
                dve.wait_ge(x_hi_ready, count(1, g, 1))
                dve.wait_ge(xn_ready, count(1, g, 1))
                if exists(after(g, -2)):
                    dve.wait_ge(hidden_ps, count(K, after(g, -2), K))
                nc.vector.tensor_tensor(x_lo[:, g[1], :], xn[:, :], x_hi[:, g[1], :].bitcast(F32), ALU.subtract) \
                    .then_inc(x_lo_ready, 1)

            def top_two(g):
                dve.wait_ge(logits_ps, count(1, g, 1))
                nc.vector.tensor_tensor(logits[:, :, :], ps_b[:, 0:T * E].rearrange("p (t e) -> p t e", e=E),
                                        br_bc[:, None, :].broadcast_to([P, T, E]), ALU.add).then_inc(logits_ready, 1)
                dve.wait_ge(ident_ready, 2)
                dve.wait_ge(logits_ready, count(1, g, 1))
                if exists(after(g, -1)):
                    dve.wait_ge(top_f_ready, count(1, after(g, -1), 1))
                    dve.wait_ge(z_ready, count(1, after(g, -1), 1))
                for t in range(T):
                    last = nc.vector.max(top_v[:, t, :], logits[:, t, :])
                last.then_inc(top_v_ready, 1)
                dve.wait_ge(top_v_ready, count(1, g, 1))
                nc.vector.tensor_tensor(gap[:, :], top_v[:, :, 1], top_v[:, :, 0], ALU.subtract)
                for t in range(T):
                    last = nc.vector.max_index(top_i[:, t, :], top_v[:, t, :], logits[:, t, :])
                last.then_inc(top_ready, 1)

            def gate_reciprocal(g):
                dve.wait_ge(z1_ready, count(1, g, 1))
                if exists(after(g, -1)):
                    dve.wait_ge(hot_ready, count(1, after(g, -1), 1))
                nc.vector.reciprocal(g1[:, :], z1[:, :]).then_inc(g1_ready, 1)

            def split_h(g, e):
                dve.wait_ge(h_hi_ready, count(E, g, e + 1))
                if e >= 4 or exists(after(g, -1)):
                    dve.wait_ge(y_ps, count(E, g, e - 3))
                nc.vector.tensor_tensor(h_lo[:, e % 4], h32[:, e % 2], h_hi[:, e % 4].bitcast(F32), ALU.subtract) \
                    .then_inc(h_lo_ready, 1)

            def gate_y(g, e):
                dve.wait_ge(y_ps, count(E, g, e + 1))
                if e % PAIR == 0:
                    dve.wait_ge(gate_loaded[e // PAIR], count(16, g, 16))
                if e == 0:
                    to = acc[:, g[1], :]
                    if exists(after(g, -2)):
                        dve.wait_ge(yT_ps, count(1, after(g, -2), 1))
                else:
                    to = gated[:, e % 2, :]
                    if e > 2 or exists(after(g, -1)):
                        dve.wait_ge(acc_ready, count(E - 1, g, max(e - 2, 0)))
                nc.vector.scalar_tensor_tensor(to, ps_y[e % 2][:, :], b2_col[:, e:e + 1], gate_bc[:, g[1], e, :],
                                               ALU.add, ALU.mult).then_inc(gated_ready, 1)

            def finish(g):
                dve.wait_ge(yT_ps, count(1, g, 1))
                if exists(after(g, -2)):
                    dve.wait_ge(stored[g[1]], 16 * g[0])
                nc.vector.tensor_tensor(out_sb[:, g[1]], ps_a[:, :].rearrange("p (t f) -> p t f", t=T), x1[:, g[1]],
                                        ALU.add).then_inc(out_ready, 1)

            def start():
                dve.wait_ge(ident_ready, 2)
                front_stats((0, 0))
                front_scale((0, 0))
                split_weights(w1_loaded, 1, W1_hi, W1_lo)
                residual((0, 0))
                center((0, 0))
                split_x((0, 0))
                dve.wait_ge(small_loaded, SMALL_LOADS)
                top_two((0, 0))
                gate_reciprocal((0, 0))
                split_weights(w2_loaded, 2, W2_hi, W2_lo)
                dve.wait_ge(setup_sb, 1)
                split_h((0, 0), 0)
                front_stats((0, 1))
                front_scale((0, 1))

            def body(g):
                nxt = after(g, 1)
                for s in range(E):
                    if s + 1 < E:
                        split_h(g, s + 1)
                    elif exists(nxt):
                        split_h(nxt, 0)
                    if s > 0:
                        gate_y(g, s - 1)
                    elif exists(after(g, -1)):
                        gate_y(after(g, -1), E - 1)
                    if s == 1 and exists(after(g, -1)):
                        finish(after(g, -1))
                    if exists(nxt):
                        if s == 2:
                            residual(nxt)
                        if s == 3:
                            center(nxt)
                        if s == 5:
                            split_x(nxt)
                            top_two(nxt)
                        if s == 6:
                            gate_reciprocal(nxt)
                    if exists(after(g, 2)):
                        if s == 6:
                            front_stats(after(g, 2))
                        if s == 7:
                            front_scale(after(g, 2))

            run(dve, start, body)
            gate_y((G // 2 - 1, 1), E - 1)
            finish((G // 2 - 1, 1))

        @block.tensor
        def _(pe):
            def layer1(g, e):
                p = g[1]
                if e == 0:
                    pe.wait_ge(x_hi_ready, count(1, g, 1))
                    pe.wait_ge(x_lo_ready, count(1, g, 1))
                for c in range(C):
                    k = C * e + c
                    if k >= HB or exists(after(g, -1)):
                        pe.wait_ge(gelu_done, count(K, g, k - HB + 1))
                    w = slice(k * P, (k + 1) * P)
                    bank = ps_h[k % HB][:, :]
                    nc.tensor.matmul(bank, W1_hi[:, w], x_hi[:, p, :], start=True, stop=False)
                    nc.tensor.matmul(bank, W1_hi[:, w], x_lo[:, p, :], start=False, stop=False)
                    nc.tensor.matmul(bank, W1_lo[:, w], x_hi[:, p, :], start=False, stop=True).then_inc(hidden_ps, 1)

            def layer2(g, e):
                bank = ps_y[e % 2][:, :]
                pe.wait_ge(h_hi_ready, count(E, g, e + 1))
                if e >= 2 or exists(after(g, -1)):
                    pe.wait_ge(gated_ready, count(E, g, e - 1))
                for c in range(C):
                    w = slice((C * e + c) * P, (C * e + c + 1) * P)
                    nc.tensor.matmul(bank, W2_hi[:, w], h_hi[:, e % 4, c, :], start=(c == 0), stop=False)
                    nc.tensor.matmul(bank, W2_lo[:, w], h_hi[:, e % 4, c, :], start=False, stop=False)
                pe.wait_ge(h_lo_ready, count(E, g, e + 1))
                for c in range(C):
                    w = slice((C * e + c) * P, (C * e + c + 1) * P)
                    last = nc.tensor.matmul(bank, W2_hi[:, w], h_lo[:, e % 4, c, :], start=False, stop=(c == C - 1))
                last.then_inc(y_ps, 1)

            def transpose_a2(g):
                pe.wait_ge(a2_ready, count(1, g, 1))
                if exists(after(g, -1)):
                    pe.wait_ge(gatesT_ready, count(1, after(g, -1), 1))
                for t in range(T):
                    last = nc.tensor.transpose(ps_a[:, t * P:(t + 1) * P], a2[:, t, :], ident[:, :])
                last.then_inc(a2T_ps, 1)

            def convolve(g):
                pe.wait_ge(xs_ready, count(1, g, 1))
                pe.wait_ge(a2T_ready, count(1, g, 1))
                if exists(after(g, -1)):
                    pe.wait_ge(logits_ready, count(1, after(g, -1), 1))
                for t in range(T):
                    c = slice(t * P, (t + 1) * P)
                    last = nc.tensor.matmul(ps_b[:, c], xs[:, t, :], a2T[:, c], start=True, stop=True)
                last.then_inc(hT_ps, 1)

            def project(g):
                pe.wait_ge(hT_ready, count(1, g, 1))
                for t in range(T):
                    c = slice(t * P, (t + 1) * P)
                    last = nc.tensor.matmul(ps_b[:, c], hT[:, c], WT[:, :], start=True, stop=True)
                last.then_inc(conv_ps, 1)

            def transpose_xc(g):
                pe.wait_ge(xc_ready, count(1, g, 1))
                for t in range(T):
                    last = nc.tensor.transpose(ps_a[:, t * P:(t + 1) * P], xc[:, t, :], ident[:, :])
                last.then_inc(xcT_ps, 1)

            def route(g):
                pe.wait_ge(xn_ready, count(1, g, 1))
                pe.wait_ge(x1_ready, count(1, g, 1))
                for t in range(T):
                    last = nc.tensor.matmul(ps_b[:, t * E:(t + 1) * E], xn[:, t * P:(t + 1) * P], Wr_sb[:, :],
                                            start=True, stop=True)
                last.then_inc(logits_ps, 1)

            def transpose_gates(g):
                pe.wait_ge(gates_ready, count(1, g, 1))
                pe.wait_ge(xn_ready, count(1, g, 1))
                nc.tensor.transpose(ps_a[:, 0:P], gates[:, :], ident[:, :]).then_inc(gatesT_ps, 1)

            def transpose_y(g):
                pe.wait_ge(acc_ready, count(E - 1, g, E - 1))
                if exists(after(g, 2)):
                    pe.wait_ge(a2T_ready, count(1, after(g, 2), 1))
                else:
                    pe.wait_ge(gatesT_ready, G)
                    pe.wait_ge(out_ready, count(1, after(g, -1), 1))
                for t in range(T):
                    c = slice(t * P, (t + 1) * P)
                    last = nc.tensor.transpose(ps_a[:, c], acc[:, g[1], c], ident[:, :])
                last.then_inc(yT_ps, 1)

            def start():
                pe.wait_ge(ident_ready, 2)
                pe.wait_ge(small_loaded, SMALL_LOADS)
                nc.tensor.transpose(ps_a[:, 0:P], small_rows[:, :], ident[:, :])
                nc.tensor.transpose(ps_a[:, P:2 * P], W_sb[:, :], ident[:, :]).then_inc(setup_ps, 1)
                pe.wait_ge(setup_sb, 1)
                transpose_a2((0, 0))
                convolve((0, 0))
                project((0, 0))
                transpose_xc((0, 0))
                route((0, 0))
                transpose_gates((0, 0))
                pe.wait_ge(w_split, 1)
                layer1((0, 0), 0)
                layer1((0, 0), 1)
                pe.wait_ge(w_split, 2)

            def body(g):
                nxt = after(g, 1)
                for s in range(E):
                    if s + 2 < E:
                        layer1(g, s + 2)
                    elif exists(nxt):
                        layer1(nxt, s + 2 - E)
                    if exists(nxt):
                        if s == 0:
                            transpose_a2(nxt)
                        if s == 1:
                            convolve(nxt)
                        if s == 2:
                            project(nxt)
                        if s == 4:
                            transpose_xc(nxt)
                        if s == 5:
                            route(nxt)
                        if s == 7:
                            transpose_gates(nxt)
                    if s == 1 and exists(after(g, -1)):
                        transpose_y(after(g, -1))
                    layer2(g, s)

            run(pe, start, body)
            transpose_y((G // 2 - 1, 1))


_INS = ['x', 'adj', 'L0_gnn_W', 'L0_gnn_b', 'L0_gnn_alpha', 'L0_ffn_gamma', 'L0_ffn_beta', 'L0_ffn_Wr', 'L0_ffn_br',
        'L0_ffn_W1', 'L0_ffn_b1', 'L0_ffn_W2', 'L0_ffn_b2']


def kernel(**inputs):
    import numpy as _np
    import concourse.bacc as _bacc
    from concourse import mybir as _mybir
    from concourse.bass_utils import run_bass_kernel_spmd as _run

    nc = _bacc.Bacc("TRN2", target_bir_lowering=False, num_devices=1)
    arrays, args = {}, []
    for name in _INS:
        a = _np.ascontiguousarray(inputs[name])
        arrays[f"in_{name}_dram"] = a
        args.append(nc.dram_tensor(f"in_{name}_dram", a.shape, _mybir.dt.from_np(a.dtype), kind="ExternalInput").ap())
    shape = inputs['x'].shape
    args.append(nc.dram_tensor("out_0_dram", shape, _mybir.dt.float32, kind="ExternalOutput").ap())
    build(nc, *args)
    r = _run(nc, [arrays], core_ids=[0])
    return r.results[0]["out_0_dram"]
```

```python
import math
from contextlib import ExitStack

import concourse.bass as bass
from concourse import mybir

F32 = mybir.dt.float32
F32R = mybir.dt.float32r
U32 = mybir.dt.uint32
ALU = mybir.AluOpType
ACT = mybir.ActivationFunctionType
AX = mybir.AxisListType

P = 128
T = 4
N = T * P
EPS = 1e-5
MIN_ALPHA = 1e-10


def after(group, n):
    half, parity = group
    return half + (parity + n) // 2, (parity + n) % 2


def number(group):
    return 2 * group[0] + group[1]


def build(nc, x, adj, W, b, alpha, gamma, beta, Wr, br, W1, b1, W2, b2, out):
    G = x.shape[0] // T
    E = W1.shape[0]
    C = W1.shape[2] // P
    K = E * C
    ROWS = K + E + 2
    HB = 2 * C
    FULL = (2, 4, 6)
    SPLIT = [e for e in range(E) if e not in FULL]
    S = len(SPLIT)
    PAIR = 2

    def exists(group):
        half, parity = group
        return not isinstance(half, int) or 0 <= 2 * half + parity < G

    def count(per_group, group, k):
        return per_group * number(group) + k

    def split_count(group, e):
        return count(S, group, SPLIT.index(e) + 1)

    x_v = x.rearrange("(g t) n f -> g n t f", t=T)
    adj_v = adj.rearrange("(g t) n m -> g n t m", t=T)
    out_v = out.rearrange("(g t) n f -> g n t f", t=T)

    ctx = ExitStack()
    with ctx:
        def sb(name, shape, dt=F32):
            return ctx.enter_context(nc.sbuf_tensor(name, shape, dt))

        def ps(name, shape):
            return ctx.enter_context(nc.psum_tensor(name, shape, F32))

        def sem(name):
            return ctx.enter_context(nc.semaphore(name))

        gates_dram = nc.dram_tensor("gates_scratch", (2, E, T, P), F32, kind="Internal").ap()

        ident = sb("ident", [P, P])
        minus_half = sb("minus_half", [P, 2 * T])
        euler = sb("euler", [P, T])
        iota_e = sb("iota_e", [P, E])
        small_rows = sb("small_rows", [P, P])
        small_cols = sb("small_cols", [P, P])
        b1_col = small_cols[:, 0:K]
        b2_col = small_cols[:, K:K + E]
        gamma_col = small_cols[:, K + E:K + E + 1]
        beta_col = small_cols[:, K + E + 1:K + E + 2]
        W_sb = sb("W_sb", [P, P])
        WT = sb("WT", [P, P])
        bias_bc = sb("bias_bc", [P, P])
        br_bc = sb("br_bc", [P, E])
        alpha_bc = sb("alpha_bc", [P, 1])
        alpha_eff = sb("alpha_eff", [P, 1])
        Wr_sb = sb("Wr_sb", [P, E])
        W2_sb = sb("W2_sb", [P, K * P])
        W1_hi = sb("W1_hi", [P, K * P], F32R)
        W1_lo = sb("W1_lo", [P, K * P], F32R)
        W2_hi = sb("W2_hi", [P, K * P], F32R)
        W2_lo = sb("W2_lo", [P, K * P], F32R)

        xt = sb("xt", [P, 2, T, P])
        at = sb("at", [P, 2, T, P])
        x_stats = sb("x_stats", [P, T, 6])
        x_mv = sb("x_mv", [P, T, 2])
        neg_mean = sb("neg_mean", [P, T])
        deg = sb("deg", [P, T])
        pow_in = sb("pow_in", [P, 2 * T])
        pow_out = sb("pow_out", [P, 2, 2 * T])
        r_d = sb("r_d", [P, T])
        neg_mean_r_d = sb("neg_mean_r_d", [P, T])
        alpha_deg = sb("alpha_deg", [P, T])
        xs = sb("xs", [P, T, P])
        a2 = sb("a2", [P, T, P])
        a2T = sb("a2T", [P, N])
        hT = sb("hT", [P, N])
        xb = sb("xb", [P, T, P])
        x1 = sb("x1", [P, 2, T, P])
        x1_stats = sb("x1_stats", [P, T, 6])
        x1_mv = sb("x1_mv", [P, T, 2])
        var2 = sb("var2", [P, T])
        neg_mean2 = sb("neg_mean2", [P, T])
        s2 = sb("s2", [P, T])
        neg_mean_s2 = sb("neg_mean_s2", [P, T])
        xc = sb("xc", [P, T, P])
        xn = sb("xn", [P, N])
        x_hi = sb("x_hi", [P, 2, N], F32R)
        x_lo = sb("x_lo", [P, 2, N], F32R)
        logits = sb("logits", [P, T, E])
        top_v = sb("top_v", [P, T, 8])
        top_i = sb("top_i", [P, T, 8], U32)
        gap = sb("gap", [P, T])
        z = sb("z", [P, T])
        z1 = sb("z1", [P, T])
        g12 = sb("g12", [P, T, 2])
        hot = sb("hot", [P, T, 2, E])
        hot_g = sb("hot_g", [P, T, 2, E])
        gates = sb("gates", [P, P])
        gatesT = sb("gatesT", [P, P])
        gate_bc = sb("gate_bc", [P, 2, E, N])
        W1_sb = gate_bc[:, 1].rearrange("p e n -> p (e n)")[:, 0:K * P]

        h32 = sb("h32", [P, 4, C, N])
        h_hi = sb("h_hi", [P, 4, C, N], F32R)
        h_lo = sb("h_lo", [P, 4, C, N], F32R)
        gated = sb("gated", [P, 2, N])
        acc = sb("acc", [P, 2, N])
        out_sb = sb("out_sb", [P, 2, T, P])

        ps_h = [ps(f"ps_h{k}", [P, N]) for k in range(HB)]
        ps_y = [ps(f"ps_y{k}", [P, N]) for k in range(2)]
        ps_a = ps("ps_a", [P, N])
        ps_b = ps("ps_b", [P, N])

        small_loaded, alpha_loaded = sem("small_loaded"), sem("alpha_loaded")
        w1_loaded, w2_loaded = sem("w1_loaded"), sem("w2_loaded")
        x_loaded = [sem(f"x_loaded{k}") for k in range(2)]
        adj_loaded = [sem(f"adj_loaded{k}") for k in range(2)]
        zeroed, ident_ready, consts_ready = sem("zeroed"), sem("ident_ready"), sem("consts_ready")
        setup_ps, setup_sb = sem("setup_ps"), sem("setup_sb")
        w_hi_done, w_split = sem("w_hi_done"), sem("w_split")
        alpha_ready = sem("alpha_ready")
        x_stats_ready, x_mv_ready = sem("x_stats_ready"), sem("x_mv_ready")
        deg_ready, pow_in_ready, pow_out_ready = sem("deg_ready"), sem("pow_in_ready"), sem("pow_out_ready")
        r_d_ready, scales_ready = sem("r_d_ready"), sem("scales_ready")
        xs_ready, a2_ready, xb_ready = sem("xs_ready"), sem("a2_ready"), sem("xb_ready")
        a2T_ps, a2T_ready = sem("a2T_ps"), sem("a2T_ready")
        hT_ps, hT_ready = sem("hT_ps"), sem("hT_ready")
        conv_ps, x1_ready = sem("conv_ps"), sem("x1_ready")
        x1_stats_ready, x1_mv_ready = sem("x1_stats_ready"), sem("x1_mv_ready")
        s2_scale_ready = sem("s2_scale_ready")
        var2_ready, s2_ready, xc_ready = sem("var2_ready"), sem("s2_ready"), sem("xc_ready")
        xcT_ps, xn_ready, x_hi_ready, x_lo_ready = sem("xcT_ps"), sem("xn_ready"), sem("x_hi_ready"), sem("x_lo_ready")
        logits_ps, logits_ready = sem("logits_ps"), sem("logits_ready")
        top_v_ready, top_ready = sem("top_v_ready"), sem("top_ready")
        z_ready, z1_ready, g1_ready, g2_ready = sem("z_ready"), sem("z1_ready"), sem("g1_ready"), sem("g2_ready")
        hot_ready, hot_g_ready, gates_ready = sem("hot_ready"), sem("hot_g_ready"), sem("gates_ready")
        gatesT_ps, gatesT_ready = sem("gatesT_ps"), sem("gatesT_ready")
        gates_stored = sem("gates_stored")
        gate_loaded = [sem(f"gate_loaded{k}") for k in range(E // PAIR)]
        hidden_ps, gelu_done = sem("hidden_ps"), sem("gelu_done")
        h_hi_ready, h_lo_ready = sem("h_hi_ready"), sem("h_lo_ready")
        y_ps, gated_ready, acc_ready = sem("y_ps"), sem("gated_ready"), sem("acc_ready")
        yT_ps, out_ready = sem("yT_ps"), sem("out_ready")
        stored = [sem(f"stored{k}") for k in range(2)]

        SMALL_LOADS = 8 * 16

        block = ctx.enter_context(nc.Block())

        def run(eng, start, body):
            start()
            body((0, 0))
            body((0, 1))
            with eng.Fori(1, G // 2 - 1) as half:
                body((half, 0))
                body((half, 1))
            body((G // 2 - 1, 0))
            body((G // 2 - 1, 1))

        @block.sync
        def _(sp):
            def load(g):
                p = g[1]
                if exists(after(g, -2)):
                    sp.wait_ge(xs_ready, count(1, after(g, -2), 1))
                    sp.wait_ge(a2_ready, count(1, after(g, -2), 1))
                    sp.wait_ge(xb_ready, count(1, after(g, -2), 1))
                sp.dma_start(xt[:, p], x_v[number(g)]).then_inc(x_loaded[p], 16)
                sp.dma_start(at[:, p], adj_v[number(g)]).then_inc(adj_loaded[p], 16)

            def spread_gates(g):
                p = g[1]
                sp.wait_ge(gatesT_ready, count(1, g, 1))
                if exists(after(g, -1)):
                    for k in range(E // PAIR):
                        sp.wait_ge(gate_loaded[k], count(16, after(g, -1), 16))
                sp.dma_start(gates_dram[p].rearrange("e t n -> t e n"), gatesT[0:T * E, :]).then_inc(gates_stored, 16)
                sp.wait_ge(gates_stored, count(16, g, 16))
                if exists(after(g, -2)):
                    sp.wait_ge(gated_ready, count(E, after(g, -2), E))
                for k in range(E // PAIR):
                    src = gates_dram[p, PAIR * k:PAIR * (k + 1)].rearrange("e t n -> (e t n)").partition_broadcast(P)
                    sp.dma_start(gate_bc[:, p, PAIR * k:PAIR * (k + 1), :].rearrange("p e n -> p (e n)"), src) \
                        .then_inc(gate_loaded[k], 16)

            def store(g):
                sp.wait_ge(out_ready, count(1, g, 1))
                sp.dma_start(out_v[number(g)], out_sb[:, g[1]]).then_inc(stored[g[1]], 16)

            def start():
                load((0, 0))
                load((0, 1))
                sp.wait_ge(small_loaded, SMALL_LOADS)
                sp.dma_start(W1_sb.rearrange("p (e h) -> p e h", e=E), W1.rearrange("e d h -> d e h")).then_inc(w1_loaded, 16)
                sp.dma_start(W2_sb[:, :].rearrange("p (k o) -> p k o", o=P),
                             W2.rearrange("e (c p) o -> p (e c) o", p=P)).then_inc(w2_loaded, 16)
                spread_gates((0, 0))

            def body(g):
                if exists(after(g, 2)):
                    load(after(g, 2))
                if exists(after(g, -1)):
                    store(after(g, -1))
                if exists(after(g, 1)):
                    spread_gates(after(g, 1))

            run(sp, start, body)
            store((G // 2 - 1, 1))
            for p in range(2):
                sp.wait_ge(stored[p], 16 * (G // 2))

        @block.gpsimd
        def _(pool):
            def degree_pow(g):
                pool.wait_ge(pow_in_ready, count(1, g, 1))
                if exists(after(g, -2)):
                    pool.wait_ge(x1_ready, count(1, after(g, -2), 1))
                nc.gpsimd.tensor_tensor(pow_out[:, g[1], :], pow_in[:, :], minus_half[:, :], ALU.pow) \
                    .then_inc(pow_out_ready, 1)
                if exists(after(g, -1)):
                    pool.wait_ge(xs_ready, count(1, after(g, -1), 1))
                    pool.wait_ge(a2_ready, count(1, after(g, -1), 1))
                pool.wait_ge(pow_out_ready, count(1, g, 1))
                nc.gpsimd.tensor_tensor(r_d[:, :], pow_out[:, g[1], 0:T], pow_out[:, g[1], T:2 * T], ALU.mult) \
                    .then_inc(r_d_ready, 1)
                nc.gpsimd.tensor_scalar(alpha_deg[:, :], pow_in[:, T:2 * T], alpha_eff[:, 0:1], None, ALU.mult)
                pool.wait_ge(r_d_ready, count(1, g, 1))
                nc.gpsimd.tensor_tensor(neg_mean_r_d[:, :], r_d[:, :], neg_mean[:, :], ALU.mult) \
                    .then_inc(scales_ready, 1)

            def add_bias(g):
                pool.wait_ge(x_loaded[g[1]], 16 * g[0] + 16)
                if exists(after(g, -1)):
                    pool.wait_ge(x1_ready, count(1, after(g, -1), 1))
                nc.gpsimd.tensor_tensor(xb[:, :, :], xt[:, g[1]], bias_bc[:, None, :].broadcast_to([P, T, P]), ALU.add) \
                    .then_inc(xb_ready, 1)

            def norm_pow(g):
                if exists(after(g, -1)):
                    pool.wait_ge(xc_ready, count(1, after(g, -1), 1))
                pool.wait_ge(var2_ready, count(1, g, 1))
                nc.gpsimd.tensor_tensor(s2[:, :], var2[:, :], minus_half[:, 0:T], ALU.pow).then_inc(s2_ready, 1)
                pool.wait_ge(s2_ready, count(1, g, 1))
                nc.gpsimd.tensor_tensor(neg_mean_s2[:, :], s2[:, :], neg_mean2[:, :], ALU.mult) \
                    .then_inc(s2_scale_ready, 1)

            def gate(g):
                pool.wait_ge(top_ready, count(1, g, 1))
                nc.gpsimd.tensor_tensor(z[:, :], euler[:, :], gap[:, :], ALU.pow).then_inc(z_ready, 1)
                pool.wait_ge(consts_ready, 1)
                pool.wait_ge(z_ready, count(1, g, 1))
                nc.gpsimd.tensor_scalar(z1[:, :], z[:, :], 1.0, None, ALU.add).then_inc(z1_ready, 1)
                pool.wait_ge(g1_ready, count(1, g, 1))
                nc.gpsimd.tensor_tensor(g12[:, :, 1], g12[:, :, 0], z[:, :], ALU.mult).then_inc(g2_ready, 1)
                pool.wait_ge(hot_ready, count(1, g, 1))
                pool.wait_ge(g2_ready, count(1, g, 1))
                nc.gpsimd.tensor_tensor(hot_g[:, :, :, :], hot[:, :, :, :],
                                        g12[:, :, :, None].broadcast_to([P, T, 2, E]), ALU.mult).then_inc(hot_g_ready, 1)
                if exists(after(g, -1)):
                    pool.wait_ge(gatesT_ps, count(1, after(g, -1), 1))
                pool.wait_ge(hot_g_ready, count(1, g, 1))
                nc.gpsimd.tensor_tensor(gates[:, 0:T * E].rearrange("p (t e) -> p t e", e=E), hot_g[:, :, 0, :],
                                        hot_g[:, :, 1, :], ALU.add).then_inc(gates_ready, 1)

            def start():
                nc.gpsimd.memset(ident[:, :], 0.0).then_inc(ident_ready, 1)
                nc.gpsimd.memset(small_rows[:, :], 0.0).then_inc(zeroed, 1)
                nc.gpsimd.memset(gates[:, :], 0.0)
                nc.gpsimd.memset(minus_half[:, :], -0.5)
                nc.gpsimd.memset(euler[:, :], math.e)
                nc.gpsimd.iota(iota_e[:, :], [[1, E]], base=0, channel_multiplier=0,
                               allow_small_or_imprecise_dtypes=True).then_inc(consts_ready, 1)
                pool.wait_ge(ident_ready, 1)
                nc.gpsimd.affine_select(out=ident[:, :], in_=ident[:, :], compare_op=ALU.not_equal, fill=1.0,
                                        base=0, pattern=[[-1, P]], channel_multiplier=1).then_inc(ident_ready, 1)
                pool.wait_ge(alpha_loaded, 16)
                nc.gpsimd.tensor_scalar(alpha_eff[:, :], alpha_bc[:, :], MIN_ALPHA, None, ALU.max).then_inc(alpha_ready, 1)
                pool.wait_ge(alpha_ready, 1)
                pool.wait_ge(consts_ready, 1)
                degree_pow((0, 0))
                pool.wait_ge(small_loaded, SMALL_LOADS)
                add_bias((0, 0))
                degree_pow((0, 1))
                norm_pow((0, 0))
                gate((0, 0))
                add_bias((0, 1))

            def body(g):
                if exists(after(g, 1)):
                    norm_pow(after(g, 1))
                if exists(after(g, 2)):
                    degree_pow(after(g, 2))
                if exists(after(g, 1)):
                    gate(after(g, 1))
                if exists(after(g, 2)):
                    add_bias(after(g, 2))

            run(pool, start, body)

        @block.scalar
        def _(act):
            def hidden(g, e):
                if e >= 4 or exists(after(g, -1)):
                    act.wait_ge(y_ps, count(E, g, e - 3))
                for c in range(C):
                    k = C * e + c
                    act.wait_ge(hidden_ps, count(K, g, k + 1))
                    nc.scalar.activation(h32[:, e % 4, c, :], ps_h[k % HB][:, :], ACT.Gelu, bias=b1_col[:, k:k + 1]) \
                        .then_inc(gelu_done, 1)

            def head(g, e):
                if e in SPLIT:
                    act.wait_ge(gelu_done, count(K, g, C * (e + 1)))
                    nc.scalar.activation(h_hi[:, e % 4], h32[:, e % 4], ACT.Copy).then_inc(h_hi_ready, 1)

            def scale_x(g):
                act.wait_ge(scales_ready, count(1, g, 1))
                if exists(after(g, -1)):
                    act.wait_ge(hT_ps, count(1, after(g, -1), 1))
                for t in range(T):
                    last = nc.scalar.activation(xs[:, t, :], xt[:, g[1], t, :], ACT.Identity,
                                                bias=neg_mean_r_d[:, t:t + 1], scale=r_d[:, t:t + 1])
                last.then_inc(xs_ready, 1)

            def scale_x1(g):
                act.wait_ge(s2_scale_ready, count(1, g, 1))
                if exists(after(g, -1)):
                    act.wait_ge(xcT_ps, count(1, after(g, -1), 1))
                for t in range(T):
                    last = nc.scalar.activation(xc[:, t, :], x1[:, g[1], t, :], ACT.Identity,
                                                bias=neg_mean_s2[:, t:t + 1], scale=s2[:, t:t + 1])
                last.then_inc(xc_ready, 1)

            def evacuate_a2T(g):
                act.wait_ge(a2T_ps, count(1, g, 1))
                if exists(after(g, -1)):
                    act.wait_ge(hT_ps, count(1, after(g, -1), 1))
                nc.scalar.activation(a2T[:, :], ps_b[:, :], ACT.Copy).then_inc(a2T_ready, 1)

            def evacuate_hT(g):
                act.wait_ge(hT_ps, count(1, g, 1))
                if exists(after(g, -1)):
                    act.wait_ge(conv_ps, count(1, after(g, -1), 1))
                nc.scalar.activation(hT[:, :], ps_b[:, :], ACT.Copy).then_inc(hT_ready, 1)

            def scale_xn(g):
                act.wait_ge(xcT_ps, count(1, g, 1))
                if exists(after(g, -1)):
                    act.wait_ge(logits_ps, count(1, after(g, -1), 1))
                    act.wait_ge(x_lo_ready, count(1, after(g, -1), 1))
                if exists(after(g, -2)):
                    act.wait_ge(hidden_ps, count(K, after(g, -2), K))
                nc.scalar.activation(xn[:, :], ps_a[:, :], ACT.Identity, bias=beta_col, scale=gamma_col) \
                    .then_inc(xn_ready, 1)
                nc.scalar.activation(x_hi[:, g[1], :], ps_a[:, :], ACT.Identity, bias=beta_col, scale=gamma_col) \
                    .then_inc(x_hi_ready, 1)

            def evacuate_gatesT(g):
                act.wait_ge(gatesT_ps, count(1, g, 1))
                if exists(after(g, -1)):
                    act.wait_ge(gates_stored, count(16, after(g, -1), 16))
                nc.scalar.activation(gatesT[:, :], ps_a[:, 0:P], ACT.Copy).then_inc(gatesT_ready, 1)

            def weights_hi(loaded, w, hi):
                act.wait_ge(loaded, 16)
                nc.scalar.activation(hi[:, :], w, ACT.Copy).then_inc(w_hi_done, 1)

            def start():
                act.dma_start(alpha_bc[:, :], alpha.partition_broadcast(P)).then_inc(alpha_loaded, 16)
                act.dma_start(W_sb[:, :], W).then_inc(small_loaded, 16)
                act.wait_ge(zeroed, 1)
                act.dma_start(small_rows[0:K, :], b1.rearrange("e (c p) -> (e c) p", p=P)).then_inc(small_loaded, 16)
                act.dma_start(small_rows[K:K + E, :], b2).then_inc(small_loaded, 16)
                act.dma_start(small_rows[K + E:K + E + 1, :], gamma.partition_broadcast(1)).then_inc(small_loaded, 16)
                act.dma_start(small_rows[K + E + 1:ROWS, :], beta.partition_broadcast(1)).then_inc(small_loaded, 16)
                act.dma_start(bias_bc[:, :], b.partition_broadcast(P)).then_inc(small_loaded, 16)
                act.dma_start(Wr_sb[:, :], Wr).then_inc(small_loaded, 16)
                act.dma_start(br_bc[:, :], br.partition_broadcast(P)).then_inc(small_loaded, 16)
                act.wait_ge(consts_ready, 1)
                nc.scalar.activation(h32[:, 0, 0, 0:T], euler[:, :], ACT.Gelu)
                scale_x((0, 0))
                evacuate_a2T((0, 0))
                act.wait_ge(setup_ps, 1)
                nc.scalar.activation(small_cols[:, :], ps_a[:, 0:P], ACT.Copy)
                nc.scalar.activation(WT[:, :], ps_a[:, P:2 * P], ACT.Copy).then_inc(setup_sb, 1)
                evacuate_hT((0, 0))
                weights_hi(w1_loaded, W1_sb, W1_hi)
                weights_hi(w2_loaded, W2_sb[:, :], W2_hi)
                act.wait_ge(setup_sb, 1)
                scale_x1((0, 0))
                scale_xn((0, 0))
                scale_x((0, 1))
                hidden((0, 0), 0)
                head((0, 0), 0)
                hidden((0, 0), 1)
                evacuate_gatesT((0, 0))
                evacuate_a2T((0, 1))
                head((0, 0), 1)

            def body(g):
                nxt = after(g, 1)
                for s in range(E):
                    to_g, to_e = (g, s + 2) if s + 2 < E else (nxt, s + 2 - E)
                    if s == 6 and exists(nxt):
                        evacuate_gatesT(nxt)
                    if exists(to_g):
                        hidden(to_g, to_e)
                    if s == 3 and exists(nxt):
                        scale_xn(nxt)
                    if exists(to_g):
                        head(to_g, to_e)
                    if s == 0 and exists(nxt):
                        evacuate_hT(nxt)
                    if s == 2 and exists(nxt):
                        scale_x1(nxt)
                    if s == 6 and exists(after(g, 2)):
                        scale_x(after(g, 2))
                    if s == 7 and exists(after(g, 2)):
                        evacuate_a2T(after(g, 2))

            run(act, start, body)

        @block.vector
        def _(dve):
            def weights_lo(loaded, n, w, hi, lo):
                dve.wait_ge(loaded, 16)
                dve.wait_ge(w_hi_done, n)
                nc.vector.tensor_tensor(lo[:, :], w, hi[:, :].bitcast(F32), ALU.subtract).then_inc(w_split, 1)

            def front_stats(g):
                p = g[1]
                dve.wait_ge(x_loaded[p], 16 * g[0] + 16)
                for t in range(T):
                    last = nc.vector.bn_stats(x_stats[:, t, :], xt[:, p, t, :])
                last.then_inc(x_stats_ready, 1)
                dve.wait_ge(adj_loaded[p], 16 * g[0] + 16)
                dve.wait_ge(x_stats_ready, count(1, g, 1))
                nc.vector.reduce_sum(deg[:, :], at[:, p], AX.X).then_inc(deg_ready, 1)
                for t in range(T):
                    last = nc.vector.bn_aggr(x_mv[:, t, :], x_stats[:, t, :])
                last.then_inc(x_mv_ready, 1)
                dve.wait_ge(deg_ready, count(1, g, 1))
                if exists(after(g, -1)):
                    dve.wait_ge(scales_ready, count(1, after(g, -1), 1))
                nc.vector.scalar_tensor_tensor(pow_in[:, T:2 * T], deg[:, :], 0.0, deg[:, :], ALU.is_equal, ALU.add)
                dve.wait_ge(x_mv_ready, count(1, g, 1))
                nc.vector.tensor_scalar(neg_mean[:, :], x_mv[:, :, 0], -1.0, None, ALU.mult)
                nc.vector.tensor_scalar(pow_in[:, 0:T], x_mv[:, :, 1], EPS, None, ALU.add).then_inc(pow_in_ready, 1)

            def front_scale(g):
                p = g[1]
                dve.wait_ge(scales_ready, count(1, g, 1))
                if exists(after(g, -1)):
                    dve.wait_ge(a2T_ps, count(1, after(g, -1), 1))
                for t in range(T):
                    last = nc.vector.scalar_tensor_tensor(a2[:, t, :], ident[:, :], alpha_deg[:, t:t + 1],
                                                          at[:, p, t, :], ALU.mult, ALU.add)
                last.then_inc(a2_ready, 1)

            def residual(g):
                p = g[1]
                dve.wait_ge(xb_ready, count(1, g, 1))
                if exists(after(g, -2)):
                    dve.wait_ge(out_ready, count(1, after(g, -2), 1))
                dve.wait_ge(conv_ps, count(1, g, 1))
                for t in range(T):
                    last = nc.vector.scalar_tensor_tensor(x1[:, p, t, :], ps_b[:, t * P:(t + 1) * P],
                                                          pow_out[:, p, T + t:T + t + 1], xb[:, t, :],
                                                          ALU.mult, ALU.add)
                last.then_inc(x1_ready, 1)
                dve.wait_ge(x1_ready, count(1, g, 1))
                for t in range(T):
                    last = nc.vector.bn_stats(x1_stats[:, t, :], x1[:, p, t, :])
                last.then_inc(x1_stats_ready, 1)
                dve.wait_ge(ident_ready, 2)
                dve.wait_ge(x1_stats_ready, count(1, g, 1))
                for t in range(T):
                    last = nc.vector.bn_aggr(x1_mv[:, t, :], x1_stats[:, t, :])
                last.then_inc(x1_mv_ready, 1)
                dve.wait_ge(x1_mv_ready, count(1, g, 1))
                if exists(after(g, -1)):
                    dve.wait_ge(s2_scale_ready, count(1, after(g, -1), 1))
                nc.vector.tensor_scalar(neg_mean2[:, :], x1_mv[:, :, 0], -1.0, None, ALU.mult)
                nc.vector.tensor_scalar(var2[:, :], x1_mv[:, :, 1], 1.0 + EPS, EPS * EPS, ALU.mult, ALU.add) \
                    .then_inc(var2_ready, 1)

            def split_x(g):
                dve.wait_ge(x_hi_ready, count(1, g, 1))
                dve.wait_ge(xn_ready, count(1, g, 1))
                if exists(after(g, -2)):
                    dve.wait_ge(hidden_ps, count(K, after(g, -2), K))
                nc.vector.tensor_tensor(x_lo[:, g[1], :], xn[:, :], x_hi[:, g[1], :].bitcast(F32), ALU.subtract) \
                    .then_inc(x_lo_ready, 1)

            def top_two(g):
                dve.wait_ge(logits_ps, count(1, g, 1))
                nc.vector.tensor_tensor(logits[:, :, :], ps_b[:, 0:T * E].rearrange("p (t e) -> p t e", e=E),
                                        br_bc[:, None, :].broadcast_to([P, T, E]), ALU.add).then_inc(logits_ready, 1)
                dve.wait_ge(ident_ready, 2)
                dve.wait_ge(logits_ready, count(1, g, 1))
                if exists(after(g, -1)):
                    dve.wait_ge(z_ready, count(1, after(g, -1), 1))
                for t in range(T):
                    last = nc.vector.max(top_v[:, t, :], logits[:, t, :])
                last.then_inc(top_v_ready, 1)
                dve.wait_ge(top_v_ready, count(1, g, 1))
                nc.vector.tensor_tensor(gap[:, :], top_v[:, :, 1], top_v[:, :, 0], ALU.subtract)
                for t in range(T):
                    last = nc.vector.max_index(top_i[:, t, :], top_v[:, t, :], logits[:, t, :])
                last.then_inc(top_ready, 1)
                dve.wait_ge(top_ready, count(1, g, 1))
                if exists(after(g, -1)):
                    dve.wait_ge(hot_g_ready, count(1, after(g, -1), 1))
                nc.vector.tensor_tensor(hot[:, :, :, :], iota_e[:, None, None, :].broadcast_to([P, T, 2, E]),
                                        top_i[:, :, 0:2, None].broadcast_to([P, T, 2, E]), ALU.is_equal) \
                    .then_inc(hot_ready, 1)

            def gate_reciprocal(g):
                dve.wait_ge(z1_ready, count(1, g, 1))
                if exists(after(g, -1)):
                    dve.wait_ge(hot_g_ready, count(1, after(g, -1), 1))
                nc.vector.reciprocal(g12[:, :, 0], z1[:, :]).then_inc(g1_ready, 1)

            def split_h(g, e):
                dve.wait_ge(h_hi_ready, split_count(g, e))
                if e >= 4 or exists(after(g, -1)):
                    dve.wait_ge(y_ps, count(E, g, e - 3))
                nc.vector.tensor_tensor(h_lo[:, e % 4], h32[:, e % 4], h_hi[:, e % 4].bitcast(F32), ALU.subtract) \
                    .then_inc(h_lo_ready, 1)

            def gate_y(g, e):
                dve.wait_ge(y_ps, count(E, g, e + 1))
                if e % PAIR == 0:
                    dve.wait_ge(gate_loaded[e // PAIR], count(16, g, 16))
                if e == 0:
                    to = acc[:, g[1], :]
                    if exists(after(g, -2)):
                        dve.wait_ge(yT_ps, count(1, after(g, -2), 1))
                else:
                    to = gated[:, e % 2, :]
                    if e > 2 or exists(after(g, -1)):
                        dve.wait_ge(acc_ready, count(E - 1, g, max(e - 2, 0)))
                nc.vector.scalar_tensor_tensor(to, ps_y[e % 2][:, :], b2_col[:, e:e + 1], gate_bc[:, g[1], e, :],
                                               ALU.add, ALU.mult).then_inc(gated_ready, 1)

            def accumulate(g, e):
                dve.wait_ge(gated_ready, count(E, g, e + 1))
                if e > 1:
                    dve.wait_ge(acc_ready, count(E - 1, g, e - 1))
                nc.vector.tensor_tensor(acc[:, g[1], :], acc[:, g[1], :], gated[:, e % 2, :], ALU.add) \
                    .then_inc(acc_ready, 1)

            def finish(g):
                dve.wait_ge(yT_ps, count(1, g, 1))
                if exists(after(g, -2)):
                    dve.wait_ge(stored[g[1]], 16 * g[0])
                nc.vector.tensor_tensor(out_sb[:, g[1]], ps_a[:, :].rearrange("p (t f) -> p t f", t=T), x1[:, g[1]],
                                        ALU.add).then_inc(out_ready, 1)

            def start():
                dve.wait_ge(ident_ready, 2)
                dve.wait_ge(consts_ready, 1)
                front_stats((0, 0))
                front_scale((0, 0))
                front_stats((0, 1))
                residual((0, 0))
                weights_lo(w1_loaded, 1, W1_sb, W1_hi, W1_lo)
                weights_lo(w2_loaded, 2, W2_sb[:, :], W2_hi, W2_lo)
                dve.wait_ge(small_loaded, SMALL_LOADS)
                split_x((0, 0))
                top_two((0, 0))
                front_scale((0, 1))
                gate_reciprocal((0, 0))
                dve.wait_ge(setup_sb, 1)
                if 0 in SPLIT:
                    split_h((0, 0), 0)

            def body(g):
                before, nxt = after(g, -1), after(g, 1)
                for s in range(E):
                    last_g, last_e = (g, s - 1) if s else (before, E - 1)
                    next_g, next_e = (g, s + 1) if s + 1 < E else (nxt, 0)
                    if s == 1 and exists(before):
                        finish(before)
                    if exists(last_g):
                        gate_y(last_g, last_e)
                    if s == 4 and exists(nxt):
                        top_two(nxt)
                    if exists(next_g) and next_e in SPLIT:
                        split_h(next_g, next_e)
                    if s == 1 and exists(nxt):
                        residual(nxt)
                    if s == 3 and exists(after(g, 2)):
                        front_stats(after(g, 2))
                    if s == 4 and exists(nxt):
                        split_x(nxt)
                        gate_reciprocal(nxt)
                    if exists(last_g) and last_e > 0:
                        accumulate(last_g, last_e)
                    if s == 5 and exists(after(g, 2)):
                        front_scale(after(g, 2))

            run(dve, start, body)
            last = (G // 2 - 1, 1)
            gate_y(last, E - 1)
            accumulate(last, E - 1)
            finish(last)

        @block.tensor
        def _(pe):
            def layer1(g, e):
                p = g[1]
                if e == 0:
                    pe.wait_ge(x_hi_ready, count(1, g, 1))
                    pe.wait_ge(x_lo_ready, count(1, g, 1))
                for c in range(C):
                    k = C * e + c
                    if k >= HB or exists(after(g, -1)):
                        pe.wait_ge(gelu_done, count(K, g, k - HB + 1))
                    w = slice(k * P, (k + 1) * P)
                    bank = ps_h[k % HB][:, :]
                    nc.tensor.matmul(bank, W1_hi[:, w], x_hi[:, p, :], start=True, stop=False)
                    nc.tensor.matmul(bank, W1_hi[:, w], x_lo[:, p, :], start=False, stop=False)
                    nc.tensor.matmul(bank, W1_lo[:, w], x_hi[:, p, :], start=False, stop=True).then_inc(hidden_ps, 1)

            def layer2(g, e):
                bank = ps_y[e % 2][:, :]
                w = [slice(k * P, (k + 1) * P) for k in range(C * e, C * (e + 1))]
                if e >= 2 or exists(after(g, -1)):
                    pe.wait_ge(gated_ready, count(E, g, e - 1))
                if e in FULL:
                    pe.wait_ge(gelu_done, count(K, g, C * (e + 1)))
                    for c in range(C):
                        last = nc.tensor.matmul(bank, W2_sb[:, w[c]], h32[:, e % 4, c, :], start=(c == 0),
                                                stop=(c == C - 1))
                else:
                    pe.wait_ge(h_hi_ready, split_count(g, e))
                    for c in range(C):
                        nc.tensor.matmul(bank, W2_hi[:, w[c]], h_hi[:, e % 4, c, :], start=(c == 0), stop=False)
                        nc.tensor.matmul(bank, W2_lo[:, w[c]], h_hi[:, e % 4, c, :], start=False, stop=False)
                    pe.wait_ge(h_lo_ready, split_count(g, e))
                    for c in range(C):
                        last = nc.tensor.matmul(bank, W2_hi[:, w[c]], h_lo[:, e % 4, c, :], start=False,
                                                stop=(c == C - 1))
                last.then_inc(y_ps, 1)

            def transpose_a2(g):
                pe.wait_ge(a2_ready, count(1, g, 1))
                if exists(after(g, -1)):
                    pe.wait_ge(logits_ready, count(1, after(g, -1), 1))
                for t in range(T):
                    last = nc.tensor.transpose(ps_b[:, t * P:(t + 1) * P], a2[:, t, :], ident[:, :])
                last.then_inc(a2T_ps, 1)

            def convolve(g):
                pe.wait_ge(xs_ready, count(1, g, 1))
                pe.wait_ge(a2T_ready, count(1, g, 1))
                for t in range(T):
                    c = slice(t * P, (t + 1) * P)
                    last = nc.tensor.matmul(ps_b[:, c], xs[:, t, :], a2T[:, c], start=True, stop=True)
                last.then_inc(hT_ps, 1)

            def project(g):
                pe.wait_ge(hT_ready, count(1, g, 1))
                for t in range(T):
                    c = slice(t * P, (t + 1) * P)
                    last = nc.tensor.matmul(ps_b[:, c], hT[:, c], WT[:, :], start=True, stop=True)
                last.then_inc(conv_ps, 1)

            def transpose_xc(g):
                pe.wait_ge(xc_ready, count(1, g, 1))
                for t in range(T):
                    last = nc.tensor.transpose(ps_a[:, t * P:(t + 1) * P], xc[:, t, :], ident[:, :])
                last.then_inc(xcT_ps, 1)

            def route(g):
                pe.wait_ge(xn_ready, count(1, g, 1))
                pe.wait_ge(x1_ready, count(1, g, 1))
                for t in range(T):
                    last = nc.tensor.matmul(ps_b[:, t * E:(t + 1) * E], xn[:, t * P:(t + 1) * P], Wr_sb[:, :],
                                            start=True, stop=True)
                last.then_inc(logits_ps, 1)

            def transpose_gates(g):
                pe.wait_ge(gates_ready, count(1, g, 1))
                pe.wait_ge(x_hi_ready, count(1, g, 1))
                nc.tensor.transpose(ps_a[:, 0:P], gates[:, :], ident[:, :]).then_inc(gatesT_ps, 1)

            def transpose_y(g):
                pe.wait_ge(acc_ready, count(E - 1, g, E - 1))
                if exists(after(g, 1)):
                    pe.wait_ge(gatesT_ready, count(1, after(g, 1), 1))
                else:
                    pe.wait_ge(out_ready, count(1, after(g, -1), 1))
                for t in range(T):
                    c = slice(t * P, (t + 1) * P)
                    last = nc.tensor.transpose(ps_a[:, c], acc[:, g[1], c], ident[:, :])
                last.then_inc(yT_ps, 1)

            def keep_warm(n):
                for _ in range(n):
                    nc.tensor.matmul(ps_y[0][:, 0:P], ident[:, :], ident[:, :], start=True, stop=True)

            def start():
                pe.wait_ge(ident_ready, 2)
                keep_warm(22)
                transpose_a2((0, 0))
                pe.wait_ge(small_loaded, SMALL_LOADS)
                nc.tensor.transpose(ps_a[:, 0:P], small_rows[:, :], ident[:, :])
                nc.tensor.transpose(ps_a[:, P:2 * P], W_sb[:, :], ident[:, :]).then_inc(setup_ps, 1)
                convolve((0, 0))
                pe.wait_ge(setup_sb, 1)
                project((0, 0))
                keep_warm(28)
                transpose_xc((0, 0))
                keep_warm(3)
                route((0, 0))
                keep_warm(3)
                pe.wait_ge(w_split, 2)
                layer1((0, 0), 0)
                layer1((0, 0), 1)
                transpose_a2((0, 1))
                transpose_gates((0, 0))

            def body(g):
                before, nxt = after(g, -1), after(g, 1)
                for s in range(E):
                    if s + 2 < E:
                        layer1(g, s + 2)
                    elif exists(nxt):
                        layer1(nxt, s + 2 - E)
                    if s == 1 and exists(before):
                        transpose_y(before)
                    if s == 1 and exists(nxt):
                        project(nxt)
                    if s == 4 and exists(nxt):
                        route(nxt)
                    if s == 6 and exists(nxt):
                        transpose_gates(nxt)
                    layer2(g, s)
                    steps = {0: convolve, 3: transpose_xc}
                    if s in steps and exists(nxt):
                        steps[s](nxt)
                    if s == 7 and exists(after(g, 2)):
                        transpose_a2(after(g, 2))

            run(pe, start, body)
            transpose_y((G // 2 - 1, 1))


_INS = ['x', 'adj', 'L0_gnn_W', 'L0_gnn_b', 'L0_gnn_alpha', 'L0_ffn_gamma', 'L0_ffn_beta', 'L0_ffn_Wr', 'L0_ffn_br',
        'L0_ffn_W1', 'L0_ffn_b1', 'L0_ffn_W2', 'L0_ffn_b2']


def kernel(**inputs):
    import numpy as _np
    import concourse.bacc as _bacc
    from concourse import mybir as _mybir
    from concourse.bass_utils import run_bass_kernel_spmd as _run

    nc = _bacc.Bacc("TRN2", target_bir_lowering=False, num_devices=1)
    arrays, args = {}, []
    for name in _INS:
        a = _np.ascontiguousarray(inputs[name])
        arrays[f"in_{name}_dram"] = a
        args.append(nc.dram_tensor(f"in_{name}_dram", a.shape, _mybir.dt.from_np(a.dtype), kind="ExternalInput").ap())
    shape = inputs['x'].shape
    args.append(nc.dram_tensor("out_0_dram", shape, _mybir.dt.float32, kind="ExternalOutput").ap())
    build(nc, *args)
    r = _run(nc, [arrays], core_ids=[0])
    return r.results[0]["out_0_dram"]
```
